# Optimizing a Trainium2 kernel written in Bass

```python
import numpy as np
import jax
import jax.numpy as jnp

def _softmax(x, axis=-1):
    return jax.nn.softmax(x, axis=axis)

def _gelu(x):
    return jax.nn.gelu(x, approximate=True)

def _silu(x):
    return jax.nn.silu(x)

def _sigmoid(x):
    return jax.nn.sigmoid(x)

def _layernorm(x, axis=-1, eps=1e-05):
    m = jnp.mean(x, axis=axis, keepdims=True)
    v = jnp.var(x, axis=axis, keepdims=True)
    return (x - m) / jnp.sqrt(v + eps)

def _scatter_add(tgt, idx, src, axis=0):
    return tgt.at[idx].add(src)

def _segment_sum(src, seg, n):
    return jax.ops.segment_sum(src, seg, n)
kernel_name = 'mk_prb_d1_jaxref_r4_0970cb'

def setup_inputs(seed: int=0):
    np.random.seed(seed)
    _w = jnp.asarray

    def _L0_attn_setup():
        import jax, jax.numpy as jnp
        import numpy as np
        B, L, D = (2, 512, 256)
        H, HD = (16, 64)
        LD = 64
        key = jax.random.key(seed)
        ks = jax.random.split(key, 6)
        s = lambda fan_in: 1.0 / np.sqrt(fan_in)
        x_bld = jax.random.normal(ks[0], (B, L, D), dtype=jnp.float32)
        Wq = jax.random.normal(ks[1], (D, H, HD), dtype=jnp.float32) * s(D)
        Wkv_down = jax.random.normal(ks[2], (D, LD), dtype=jnp.float32) * s(D)
        Wk_up = jax.random.normal(ks[3], (LD, H, HD), dtype=jnp.float32) * s(LD)
        Wv_up = jax.random.normal(ks[4], (LD, H, HD), dtype=jnp.float32) * s(LD)
        Wout = jax.random.normal(ks[5], (H, HD, D), dtype=jnp.float32) * s(H * HD)
        return {'x_bld': x_bld, 'Wq': Wq, 'Wkv_down': Wkv_down, 'Wk_up': Wk_up, 'Wv_up': Wv_up, 'Wout': Wout}
    _L0_attn_in = _L0_attn_setup()

    def _L0_ffn_setup():
        import jax, jax.numpy as jnp
        import numpy as np
        D_MODEL = 256
        key = jax.random.key(seed)
        k_x, k_w, k_a1, k_a2 = jax.random.split(key, 4)
        x = jax.random.normal(k_x, (4, 512, D_MODEL), dtype=jnp.float32)
        weight = jax.random.normal(k_w, (D_MODEL, D_MODEL), dtype=jnp.float32) * 0.02
        aux_weight1 = jax.random.normal(k_a1, (D_MODEL, D_MODEL), dtype=jnp.float32) * 0.02
        aux_weight2 = jax.random.normal(k_a2, (D_MODEL, D_MODEL), dtype=jnp.float32) * 0.02
        bias = jnp.zeros((D_MODEL,), dtype=jnp.float32)
        return {'x': x, 'weight': weight, 'aux_weight1': aux_weight1, 'aux_weight2': aux_weight2, 'bias': bias}
    _L0_ffn_in = _L0_ffn_setup()
    _d = {'L0_attn_x_bld': _L0_attn_in['x_bld'], 'L0_attn_Wq': _L0_attn_in['Wq'], 'L0_attn_Wkv_down': _L0_attn_in['Wkv_down'], 'L0_attn_Wk_up': _L0_attn_in['Wk_up'], 'L0_attn_Wv_up': _L0_attn_in['Wv_up'], 'L0_attn_Wout': _L0_attn_in['Wout'], 'L0_ffn_weight': _L0_ffn_in['weight'], 'L0_ffn_aux_weight1': _L0_ffn_in['aux_weight1'], 'L0_ffn_aux_weight2': _L0_ffn_in['aux_weight2'], 'L0_ffn_bias': _L0_ffn_in['bias']}
    _x0 = _d['L0_attn_x_bld']
    _d['L0_attn_x_bld'] = jax.random.normal(jax.random.fold_in(jax.random.key(seed), 1), (8, 1024, 256), dtype=_x0.dtype)
    del _x0
    return _d

def reference(L0_attn_x_bld, L0_attn_Wq, L0_attn_Wkv_down, L0_attn_Wk_up, L0_attn_Wv_up, L0_attn_Wout, L0_ffn_weight, L0_ffn_aux_weight1, L0_ffn_aux_weight2, L0_ffn_bias):

    def _L0_attn_ref(x_bld, Wq, Wkv_down, Wk_up, Wv_up, Wout):
        import jax, jax.numpy as jnp
        import numpy as np
        B, L, D = (2, 512, 256)
        H, HD = (16, 64)
        LD = 64
        q_blhd = jnp.einsum('bld,dhk->blhk', x_bld, Wq)
        latent_bll = jnp.einsum('bld,dc->blc', x_bld, Wkv_down)
        k_blhd = jnp.einsum('blc,chk->blhk', latent_bll, Wk_up)
        v_blhd = jnp.einsum('blc,chk->blhk', latent_bll, Wv_up)
        attn = jnp.einsum('bqhd,bkhd->bhqk', q_blhd, k_blhd) / jnp.sqrt(jnp.asarray(HD, dtype=x_bld.dtype))
        l = x_bld.shape[1]
        mask = (jnp.arange(l)[None, :] <= jnp.arange(l)[:, None])[None, None]
        neg_inf = jnp.finfo(attn.dtype).min
        attn = jax.nn.softmax(jnp.where(mask, attn, neg_inf), axis=-1)
        y_blhd = jnp.einsum('bhqk,bkhd->bqhd', attn, v_blhd)
        return jnp.einsum('bqhd,hdo->bqo', y_blhd, Wout)

    def _L0_ffn_ref(x, weight, aux_weight1, aux_weight2, bias):
        import jax, jax.numpy as jnp
        import numpy as np
        D_MODEL = 256
        h = jnp.einsum('btc,cd->btd', x, weight)
        h = jnp.einsum('btc,cd->btd', h, aux_weight1)
        h = jnp.einsum('btc,cd->btd', h, aux_weight2)
        return jnp.tanh(h + bias)
    x = L0_attn_x_bld
    xn = _layernorm(x, axis=-1)
    x = x + _L0_attn_ref(xn, L0_attn_Wq, L0_attn_Wkv_down, L0_attn_Wk_up, L0_attn_Wv_up, L0_attn_Wout) + _L0_ffn_ref(xn, L0_ffn_weight, L0_ffn_aux_weight1, L0_ffn_aux_weight2, L0_ffn_bias)
    return x

_drawn_inputs = setup_inputs


def setup_inputs(seed=0):
    import zlib

    import numpy as np

    out = dict(_drawn_inputs(seed))
    spreads = {'L0_ffn_bias': (0.0, 0.1)}
    factors = {}
    for name, (base, spread) in spreads.items():
        noise = np.random.default_rng([zlib.crc32(name.encode()), seed]).standard_normal(out[name].shape)
        drawn = base * np.exp(spread * noise) if base else spread * noise
        out[name] = jnp.asarray(drawn.astype(out[name].dtype))
    for name, factor in factors.items():
        out[name] = (out[name] * factor).astype(out[name].dtype)
    return out
```

```python
from contextlib import ExitStack

import concourse.bass as bass
from concourse import mybir

ALU = mybir.AluOpType
ACT = mybir.ActivationFunctionType
AX = mybir.AxisListType
F32 = mybir.dt.float32
F32R = mybir.dt.float32r

P = 128
BANK = 512
LATENT = 64
HEADS, HD = 16, 64
OCTET = 8
OCTETS = HEADS // OCTET
PAIRS = OCTET // 2
LOWEST = -3.0e38
EPS = 1e-5

SEGMENT_BLOCKS = [[3, 7, 4, 0], [5, 6, 2, 1]]
PLACE = {0: 0, 3: 1, 4: 2, 7: 3, 1: 0, 2: 1, 5: 2, 6: 3}
BLOCKS = 8
SEGMENTS = 2 * OCTETS
UNITS = 4 * SEGMENTS
STEPS = OCTETS * BLOCKS * (BLOCKS + 1) // 2
SEG_STEPS = STEPS // SEGMENTS
AHEAD = 2
LAG = 2
ST_BANKS, PT_SLOTS, Y_SLOTS = 3, 4, 3


def block_of(unit):
    return SEGMENT_BLOCKS[unit // 4 % 2][unit % 4]


def segment_kind(block):
    return 0 if block in SEGMENT_BLOCKS[0] else 1


def octet_of(unit):
    return unit % UNITS // OCTET


def first_step(unit):
    n, r = divmod(unit, UNITS)
    return n * STEPS + sum(block_of(u) + 1 for u in range(r))


def key_block(unit, s):
    return block_of(unit) if s == 0 else s - 1


def max_chunks(unit):
    keys = (block_of(unit) + 1) * P
    cuts = [(0, min(keys, BANK))] + ([(BANK, keys - BANK)] if keys > BANK else [])
    return [(unit, h, k0, w) for h in range(OCTET) for k0, w in cuts]


def body_plan(batches):
    n_steps = batches * STEPS
    slots = [[] for _ in range(n_steps + 10)]
    due = [[] for _ in slots]
    for b in range(batches):
        for s in range(SEGMENTS):
            at = b * STEPS + s * SEG_STEPS
            for j in range(PAIRS):
                due[at + j].append(("Q", (b * SEGMENTS + s + 1, j)))
            if s < 2:
                for k, i in enumerate(SEGMENT_BLOCKS[s]):
                    due[at + 4 + k].append(("F", (b, i)))
                    due[at + 6 + k].append(("FA", (b, i)))
        at = b * STEPS + 2 * SEG_STEPS
        due[at + 1].append(("LN1", b + 1))
        due[at + 3].append(("LN2", b + 1))
        due[at + 5].append(("LN3", b + 1))
        for k in range(4):
            due[at + 8 + k].append(("T", (b + 1, k // 2, k % 2)))
        for k in range(2):
            due[at + 12 + k].append(("K", (b + 1, k)))
        due[at + 15].append(("KN", b + 1))
    for u in range(batches * UNITS):
        last = first_step(u) + block_of(u)
        due[last + 4].append(("R", u))
        for k in range(4):
            due[last + 5 + k].append(("RC", (u, k)))
        due[last + 9].append(("O", u))
    stream = [c for u in range(AHEAD, batches * UNITS + AHEAD) for c in max_chunks(u)]
    sent = n = 0
    step_of = [(u, s) for u in range(batches * UNITS) for s in range(block_of(u) + 1)]
    for t, slot in enumerate(slots):
        if t < n_steps:
            slot.append(("ST", (t, *step_of[t])))
        maxima, turns = [], []
        while n < len(stream) and sent < OCTET * P * (t + 1):
            maxima.append(("MAX", stream[n]))
            sent += stream[n][3]
            n += 1
            if n == len(stream) or stream[n][0] != stream[n - 1][0]:
                turns.append(("MT", stream[n - 1][0]))
        for item in turns:
            due[t + 1].insert(0, item)
        half = len(maxima) // 2
        slot += maxima[:half] + due[t] + maxima[half:]
        if LAG <= t < n_steps + LAG:
            slot.append(("PV", (t - LAG, *step_of[t - LAG])))
    return [item for slot in slots for item in slot]


def first_plan():
    plan = [("LN1", 0), ("LN2", 0), ("LN3", 0)]
    plan += [("T", (0, k // 2, k % 2)) for k in range(4)]
    plan += [("K", (0, 0)), ("K", (0, 1)), ("KN", 0)]
    plan += [("Q", (0, j)) for j in range(PAIRS)]
    for u in range(AHEAD):
        plan += [("MAX", c) for c in max_chunks(u)] + [("MT", u)]
    return plan


P0_ITEMS = ("T", "K", "KN", "Q")
P1_ITEMS = ("MT", "R", "O", "F")


class Count:

    def __init__(self, plan):
        self.at = {}
        n = {}
        for kind, key in plan:
            group = "P0" if kind in P0_ITEMS else "P1" if kind in P1_ITEMS else kind
            for name in {group, kind}:
                self.at[name, kind, key] = n.get(name, 0)
                n[name] = n.get(name, 0) + 1

    def has(self, kind, key):
        return (kind, kind, key) in self.at

    def of(self, kind, key):
        return self.at[kind, kind, key]

    def p0(self, kind, key):
        return self.at["P0", kind, key]

    def p1(self, kind, key):
        return self.at["P1", kind, key]


def build(nc, x, Wq, Wkv_down, Wk_up, Wv_up, Wout, weight, aux1, aux2, bias, out):
    B, L, D = x.shape
    C = D // P
    IN_BODY = 2
    HALF = 4 * P
    assert L == BLOCKS * P and D == 256 and B % IN_BODY == 0

    ctx = ExitStack()
    with ctx:
        def sb(name, shape, dt=F32):
            return ctx.enter_context(nc.sbuf_tensor(name, shape, dt))

        names = []

        def sem(name):
            names.append(ctx.enter_context(nc.semaphore(name)))
            return names[-1]

        q_hi = [sb(f"q_hi{i}", [P, OCTET, HALF], F32R) for i in range(2)]
        q_lo = [sb(f"q_lo{i}", [LATENT + 1, OCTET, HALF], F32R) for i in range(2)]
        k_hilo = [sb(f"k_hilo{i}", [P, L], F32R) for i in range(2)]
        k_ones = [sb(f"k_ones{i}", [LATENT + 1, L], F32R) for i in range(2)]
        latent = [sb(f"latent{i}", [P, BLOCKS, LATENT]) for i in range(2)]
        probs = sb("probs", [P, PT_SLOTS, 2 * BANK])
        p_sum = sb("p_sum", [P, 2, 2 * BANK])
        x_in = sb("x_in", [P, BLOCKS, D])
        xn = sb("xn", [P, BLOCKS, D])
        acc = sb("acc", [P, BLOCKS, D])
        xT_hi = sb("xT_hi", [P, C, L], F32R)
        xT_lo = sb("xT_lo", [P, C, L], F32R)
        y = sb("y", [P, Y_SLOTS, BANK])
        norm = sb("norm", [P, Y_SLOTS, BANK])
        wqk_hi = sb("wqk_hi", [P, C, HEADS * LATENT], F32R)
        wqk_lo = sb("wqk_lo", [P, C, HEADS * LATENT], F32R)
        wvo = sb("wvo", [P, HEADS // 2, D])
        wff_hi = sb("wff_hi", [P, C, D], F32R)
        wff_lo = sb("wff_lo", [P, C, D], F32R)
        wkv_hi = sb("wkv_hi", [P, C, 2 * LATENT], F32R)
        wkv_lo = sb("wkv_lo", [P, C, 2 * LATENT], F32R)
        bias_all = sb("bias_all", [P, D])
        ident = sb("ident", [P, P])
        ident_f = sb("ident_f", [P, LATENT])
        ident2 = sb("ident2", [P, LATENT], F32R)
        ones = sb("ones", [P, LATENT])
        causal = sb("causal", [P, L])
        maxima = sb("maxima", [P, 4, OCTET])
        maxima0 = sb("maxima0", [P, 4, OCTET])
        neg_rows = sb("neg_rows", [OCTET, 4, P], F32R)
        ff = sb("ff", [P, 4, D])
        stats = sb("stats", [P, BLOCKS, 6])
        mean_var = sb("mean_var", [P, BLOCKS, 2])
        ln = sb("ln", [P, 5, BLOCKS])

        ps = ctx.enter_context(nc.psum_tensor("ps", [P, 8, BANK], F32))
        st_bank = [ps[:, i, :] for i in range(ST_BANKS)]
        max_bank = [ps[:, ST_BANKS + i, :] for i in range(2)]
        y_bank, p0_bank, p1_bank = ps[:, 5, :], ps[:, 6, :], ps[:, 7, :]

        loaded = sem("loaded")
        dve_did = sem("dve_did")
        pe_did = sem("pe_did")
        pool_did = sem("pool_did")
        x_loaded = sem("x_loaded")
        ln_chain = sem("ln_chain")
        var_ready = sem("var_ready")
        sqrt_done = sem("sqrt_done")
        xn_ready = sem("xn_ready")
        p0_full = sem("p0_full")
        p0_hi = sem("p0_hi")
        p0_free = sem("p0_free")
        q_twice = [sem(f"q_twice{j}") for j in range(PAIRS)]
        max_full = sem("max_full")
        max_free = sem("max_free")
        max_joined = sem("max_joined")
        row_ready = sem("row_ready")
        row_placed = [sem(f"row_placed{i}") for i in range(4)]
        st_full = sem("st_full")
        exp_done = sem("exp_done")
        pool_done = sem("pool_done")
        pv_done = sem("pv_done")
        y_copied = sem("y_copied")
        p1_full = sem("p1_full")
        p1_free = sem("p1_free")
        recip_done = sem("recip_done")
        y_normal = sem("y_normal")
        tanh_done = sem("tanh_done")
        ff_added = sem("ff_added")
        stored = [sem(f"stored{s}") for s in range(2)]

        wq_in = probs[:, 0:2, :].rearrange("p a n -> p (a n)").rearrange("p (c n) -> p c n", c=C)
        wqT = probs[:, 2:4, :].rearrange("p a n -> p (a n)").rearrange("p (j d) -> p j d", d=D)
        wk_in, wv_in = p_sum[0:LATENT, 0, :], p_sum[0:LATENT, 1, :]
        acc_flat = acc[:, :, :].rearrange("p a n -> p (a n)")
        wkT = acc_flat[:, 0:512].rearrange("p (j n) -> p j n", n=LATENT)
        wvT = acc_flat[:, 512:1024].rearrange("p (j n) -> p j n", n=LATENT)
        aux12 = acc_flat[:, 1024:1536].rearrange("p (c n) -> p c n", c=C)
        wT = acc_flat[:, 1536:2048].rearrange("p (c n) -> p c n", c=C)
        wout_in = xn
        w_in = y[:, 0, :].rearrange("p (c n) -> p c n", c=C)
        aux1_in = y[:, 1, :].rearrange("p (c n) -> p c n", c=C)
        aux2_in = y[:, 2, :].rearrange("p (c n) -> p c n", c=C)
        aux1T = norm[:, 0, :].rearrange("p (c n) -> p c n", c=C)
        wkv_in = norm[:, 1, 0:C * LATENT].rearrange("p (c n) -> p c n", c=C)

        with nc.Block() as block:

            @block.sync
            def _(sp):
                for dst, src in (
                    (wq_in, Wq.rearrange("(c p) h k -> p c (h k)", p=P)),
                    (wk_in, Wk_up.rearrange("c h k -> c (h k)")),
                    (wv_in, Wv_up.rearrange("c h k -> c (h k)")),
                    (aux1_in, aux1.rearrange("(c p) n -> p c n", p=P)),
                    (w_in, weight.rearrange("(c p) n -> p c n", p=P)),
                    (aux2_in, aux2.rearrange("(c p) n -> p c n", p=P)),
                    (wout_in[:, :, :], Wout.rearrange("(j a) k o -> (a k) j o", a=2)),
                    (wkv_in, Wkv_down.rearrange("(c p) n -> p c n", p=P)),
                    (bias_all[:, :], bias.rearrange("(a n) -> a n", a=1).broadcast_to([P, D])),
                    (x_in[:, :, :], x[0].rearrange("(i p) d -> p i d", p=P)),
                ):
                    sp.dma_start(dst, src).then_inc(loaded, 16)
                sp.wait_ge(loaded, 160)

            @block.gpsimd
            def _(pool):
                nc.gpsimd.memset(ident[:, :], 0.0).then_inc(pool_did, 1)
                nc.gpsimd.memset(ident_f[:, :], 0.0).then_inc(pool_did, 1)
                nc.gpsimd.memset(causal[:, :], 0.0).then_inc(pool_did, 1)
                pool.wait_ge(pool_did, 3)
                nc.gpsimd.affine_select(
                    out=ident[:, :], in_=ident[:, :], pattern=[[-1, P]], compare_op=ALU.not_equal,
                    fill=1.0, base=0, channel_multiplier=1).then_inc(pool_did, 1)
                nc.gpsimd.affine_select(
                    out=ident_f[:, :], in_=ident_f[:, :], pattern=[[-1, LATENT]],
                    compare_op=ALU.not_equal, fill=1.0, base=0, channel_multiplier=1,
                ).then_inc(pool_did, 1)
                pool.wait_ge(pool_did, 5)
                nc.gpsimd.affine_select(
                    out=ident_f[:, :], in_=ident_f[:, :], pattern=[[-1, LATENT]],
                    compare_op=ALU.not_equal, fill=1.0, base=-LATENT, channel_multiplier=1,
                ).then_inc(pool_did, 1)
                nc.gpsimd.affine_select(
                    out=causal[:, L - P:L], in_=causal[:, L - P:L], pattern=[[-1, P]],
                    compare_op=ALU.is_ge, fill=LOWEST, base=0, channel_multiplier=1,
                ).then_inc(pool_did, 1)

            @block.tensor
            def _(pe):
                pe.wait_ge(loaded, 160)
                pe.wait_ge(pool_did, 7)
                for j in range(HEADS // 2):
                    for c in range(C):
                        at = (j % 2) * D + c * P
                        nc.tensor.transpose(ps[:, j // 2, at:at + P], wq_in[:, c, j * P:(j + 1) * P],
                                            ident[:, :]).then_inc(pe_did, 1)
                for n, w in ((4, wk_in), (5, wv_in)):
                    for j in range(HEADS // 2):
                        nc.tensor.transpose(ps[:, n, j * LATENT:(j + 1) * LATENT],
                                            w[:, j * P:(j + 1) * P],
                                            ident[0:LATENT, 0:LATENT]).then_inc(pe_did, 1)
                for n, w in ((6, aux1_in), (7, w_in)):
                    for k in range(C):
                        for c in range(C):
                            at = k * D + c * P
                            nc.tensor.transpose(ps[:, n, at:at + P], w[:, c, k * P:(k + 1) * P],
                                                ident[:, :]).then_inc(pe_did, 1)
                pe.wait_ge(dve_did, 8)
                for c in range(C):
                    for k in range(C):
                        nc.tensor.matmul(ps[:, 0, c * D:(c + 1) * D], aux1T[:, k, c * P:(c + 1) * P],
                                         aux2_in[:, k, :], start=(k == 0),
                                         stop=(k == C - 1)).then_inc(pe_did, 1)
                for c in range(C):
                    for h in range(HEADS):
                        r = (h % 2) * HD
                        at = (h // 2) * LATENT
                        nc.tensor.matmul(ps[:, 2 + 2 * c + h % 2, at:at + LATENT],
                                         wqT[r:r + HD, h // 2, c * P:(c + 1) * P],
                                         wkT[r:r + HD, h // 2, :], start=True,
                                         stop=True).then_inc(pe_did, 1)
                for h in range(OCTET):
                    r = (h % 2) * HD
                    at = (h // 2 % 2) * D
                    nc.tensor.matmul(ps[r:r + LATENT, 6 + h // 4, at:at + D],
                                     wvT[r:r + HD, h // 2, :], wout_in[r:r + HD, h // 2, :],
                                     start=True, stop=True).then_inc(pe_did, 1)
                pe.wait_ge(dve_did, 8 + 1 + 8 + 2)
                for c in range(C):
                    for k in range(C):
                        nc.tensor.matmul(ps[:, 1, c * D:(c + 1) * D], wT[:, k, c * P:(c + 1) * P],
                                         aux12[:, k, :], start=(k == 0),
                                         stop=(k == C - 1)).then_inc(pe_did, 1)
                for h in range(OCTET, HEADS):
                    r = (h % 2) * HD
                    at = (h // 2 % 2) * D
                    nc.tensor.matmul(ps[r:r + LATENT, 4 + h // 4, at:at + D],
                                     wvT[r:r + HD, h // 2, :], wout_in[r:r + HD, h // 2, :],
                                     start=True, stop=True).then_inc(pe_did, 1)

            @block.vector
            def _(dve):
                turned = HEADS // 2 * C + HEADS + 2 * C * C
                pe_first = turned + C * C + C * HEADS + OCTET
                dve.wait_ge(pe_did, turned)
                wqT_flat = wqT.rearrange("p j d -> p (j d)")
                for n in range(4):
                    nc.vector.tensor_copy(wqT_flat[:, n * BANK:(n + 1) * BANK],
                                          ps[:, n, :]).then_inc(dve_did, 1)
                nc.vector.tensor_copy(acc_flat[:, 0:512], ps[:, 4, :]).then_inc(dve_did, 1)
                nc.vector.tensor_copy(acc_flat[:, 512:1024], ps[:, 5, :]).then_inc(dve_did, 1)
                nc.vector.tensor_copy(norm[:, 0, :], ps[:, 6, :]).then_inc(dve_did, 1)
                nc.vector.tensor_copy(acc_flat[:, 1536:2048], ps[:, 7, :]).then_inc(dve_did, 1)
                dve.wait_ge(pe_did, pe_first)
                nc.vector.tensor_copy(acc_flat[:, 1024:1536], ps[:, 0, :]).then_inc(dve_did, 1)
                done = 9
                for c in range(C):
                    for g in range(2):
                        hi, lo = (w[:, c, :].rearrange("p (j g n) -> p j g n", g=2, n=LATENT)
                                  [:, :, g, :] for w in (wqk_hi, wqk_lo))
                        bank = ps[:, 2 + 2 * c + g, :].rearrange("p (j n) -> p j n", n=LATENT)
                        nc.vector.tensor_scalar(hi, bank, HD ** -0.5, None,
                                                ALU.mult).then_inc(dve_did, 1)
                        done += 1
                        dve.wait_ge(dve_did, done)
                        nc.vector.scalar_tensor_tensor(
                            out=lo, in0=bank, scalar=HD ** -0.5,
                            in1=hi.bitcast(F32), op0=ALU.mult,
                            op1=ALU.subtract).then_inc(dve_did, 1)
                        done += 1
                for n in range(2):
                    nc.vector.tensor_copy(wvo[:, 2 * n:2 * n + 2, :].rearrange("p j d -> p (j d)"),
                                          ps[:, 6 + n, :]).then_inc(dve_did, 1)
                    done += 1
                dve.wait_ge(pe_did, pe_first + C * C + OCTET)
                for n in range(2):
                    nc.vector.tensor_copy(
                        wvo[:, 4 + 2 * n:6 + 2 * n, :].rearrange("p j d -> p (j d)"),
                        ps[:, 6 + n, :]).then_inc(dve_did, 1)
                    done += 1
                wff_hi_flat = wff_hi[:, :, :].rearrange("p c n -> p (c n)")
                nc.vector.tensor_copy(wff_hi_flat, ps[:, 1, :]).then_inc(dve_did, 1)
                dve.wait_ge(dve_did, done + 1)
                nc.vector.tensor_tensor(wff_lo[:, :, :].rearrange("p c n -> p (c n)"), ps[:, 1, :],
                                        wff_hi_flat.bitcast(F32), ALU.subtract).then_inc(dve_did, 1)
                for r in range(2):
                    cols = slice(r * LATENT, (r + 1) * LATENT)
                    nc.vector.tensor_copy(wkv_hi[:, :, cols], wkv_in).then_inc(dve_did, 1)
                    dve.wait_ge(dve_did, done + 3 + 2 * r)
                    nc.vector.tensor_tensor(wkv_lo[:, :, cols], wkv_in,
                                            wkv_hi[:, :, cols].bitcast(F32),
                                            ALU.subtract).then_inc(dve_did, 1)
                nc.vector.tensor_copy(ident2[:, :], ident_f[:, :]).then_inc(dve_did, 1)
                nc.vector.memset(ones[:, :], 1.0).then_inc(dve_did, 1)
                for i in range(2):
                    nc.vector.tensor_scalar(k_ones[i][LATENT:LATENT + 1, :], causal[64:65, :], 0.0,
                                            1.0, ALU.mult, ALU.add).then_inc(dve_did, 1)

        nc.all_engine_barrier(sems_to_clear=range(names[0].num, names[-1].num + 1))

        def x_blocks(xT, c, seg):
            v = xT[:, c, :].rearrange("p (a b q) -> p a b q", a=2, b=4)
            return v[:, :, 0:4:3, :] if seg % 2 == 0 else v[:, :, 1:3, :]

        def columns(unit):
            return slice(PLACE[block_of(unit)] * P, (PLACE[block_of(unit)] + 1) * P)

        def tensor_program(pe, plan):
            count = Count(plan)
            n_max = n_p0 = n_p1 = 0

            def three_passes(dst, weights, moving):
                terms = [(a, b, c) for c in range(C) for a, b in ((0, 0), (0, 1), (1, 0))]
                for n, (a, b, c) in enumerate(terms):
                    last = nc.tensor.matmul(dst, weights(a, c), moving(b, c), start=(n == 0),
                                            stop=(n == len(terms) - 1))
                return last

            def p0_ready():
                if n_p0:
                    pe.wait_ge(p0_free, n_p0)

            def p1_ready():
                if n_p1:
                    pe.wait_ge(p1_free, n_p1)

            for kind, key in plan:
                if kind == "ST":
                    t, unit, s = key
                    kb = key_block(unit, s)
                    seg, par = unit // 4 % 2, unit // UNITS % 2
                    blk = slice(kb * P, (kb + 1) * P)
                    if s == 0 and count.has("MT", unit):
                        n = count.of("MT", unit)
                        pe.wait_ge(row_placed[n % 4], 16 * (n // 4 + 1))
                    for g in range(2):
                        n = 2 * t + g
                        if n >= ST_BANKS:
                            pe.wait_ge(exp_done, n - ST_BANKS + 1)
                        bank = st_bank[n % ST_BANKS]
                        nc.tensor.matmul(bank, k_hilo[par][:, blk],
                                         q_hi[seg][:, g:OCTET:2, columns(unit)],
                                         start=True, stop=False)
                        nc.tensor.matmul(bank, k_ones[par][:, blk],
                                         q_lo[seg][:, g:OCTET:2, columns(unit)],
                                         start=False, stop=True).then_inc(st_full, 1)
                elif kind == "PV":
                    t, unit, s = key
                    par = unit // UNITS % 2
                    for g in range(2):
                        if s == 0:
                            pe.wait_ge(pool_done, 2 * t + g + 1)
                            if unit > 0:
                                pe.wait_ge(y_copied, unit)
                        else:
                            pe.wait_ge(exp_done, 2 * t + g + 1)
                        last = nc.tensor.matmul(y_bank[g * LATENT:(g + 1) * LATENT, :],
                                                latent[par][:, key_block(unit, s), :],
                                                probs[:, t % PT_SLOTS, g * BANK:(g + 1) * BANK],
                                                start=(s == 0), stop=(s == block_of(unit)))
                    last.then_inc(pv_done, 1)
                elif kind == "MAX":
                    unit, h, k0, w = key
                    seg, par = unit // 4, unit // UNITS % 2
                    if n_max >= 2:
                        pe.wait_ge(max_free, n_max - 1)
                    if count.has("Q", (seg, h // 2)):
                        n = count.of("Q", (seg, h // 2))
                        pe.wait_ge(q_twice[h // 2], 32 * (n // PAIRS + 1))
                    nc.tensor.matmul(max_bank[n_max % 2][:, 0:w], q_hi[seg % 2][:, h, columns(unit)],
                                     k_hilo[par][:, k0:k0 + w], start=True,
                                     stop=True).then_inc(max_full, 1)
                    n_max += 1
                elif kind == "MT":
                    p1_ready()
                    if block_of(key) < 4:
                        pe.wait_ge(max_free, n_max_of[key])
                    else:
                        pe.wait_ge(max_joined, count_joined(plan, key))
                    nc.tensor.transpose(p1_bank[0:OCTET, 0:P], maxima[:, key % 4, :],
                                        ident[:, :]).then_inc(p1_full, 1)
                    n_p1 += 1
                elif kind == "R":
                    p1_ready()
                    last_step = first_step(key) + block_of(key)
                    pe.wait_ge(pool_done, 2 * last_step + 2)
                    for g in range(2):
                        part = slice(g * BANK, (g + 1) * BANK)
                        src = (probs[:, last_step % PT_SLOTS, part] if block_of(key) == 0
                               else p_sum[:, key % 2, part])
                        last = nc.tensor.matmul(p1_bank[g * LATENT:(g + 1) * LATENT, :], ones[:, :],
                                                src, start=True, stop=True)
                    last.then_inc(p1_full, 1)
                    n_p1 += 1
                elif kind == "O":
                    p1_ready()
                    pe.wait_ge(y_normal, key + 1)
                    for j in range(PAIRS):
                        last = nc.tensor.matmul(p1_bank[:, 0:D], norm[:, key % Y_SLOTS, j * P:(j + 1) * P],
                                                wvo[:, octet_of(key) * PAIRS + j, :],
                                                start=(j == 0), stop=(j == PAIRS - 1))
                    last.then_inc(p1_full, 1)
                    n_p1 += 1
                elif kind == "F":
                    p1_ready()
                    tok = slice(key[1] * P, (key[1] + 1) * P)
                    three_passes(p1_bank[:, 0:D], lambda a, c: (xT_hi, xT_lo)[a][:, c, tok],
                                 lambda b, c: (wff_hi, wff_lo)[b][:, c, :]).then_inc(p1_full, 1)
                    n_p1 += 1
                elif kind == "T":
                    p0_ready()
                    b, c, half = key
                    pe.wait_ge(xn_ready, count.of("LN3", b) + 1)
                    for k in range(4):
                        last = nc.tensor.transpose(p0_bank[:, k * P:(k + 1) * P],
                                                   xn[:, 4 * half + k, c * P:(c + 1) * P],
                                                   ident[:, :])
                    last.then_inc(p0_full, 1)
                    n_p0 += 1
                elif kind == "K":
                    p0_ready()
                    tok = slice(key[1] * HALF, (key[1] + 1) * HALF)
                    three_passes(p0_bank, lambda a, c: (wkv_hi, wkv_lo)[a][:, c, :],
                                 lambda b, c: (xT_hi, xT_lo)[b][:, c, tok]).then_inc(p0_full, 1)
                    n_p0 += 1
                elif kind == "KN":
                    p0_ready()
                    for kb in range(BLOCKS):
                        last = nc.tensor.matmul(p0_bank[:, kb * LATENT:(kb + 1) * LATENT],
                                                k_hilo[key % 2][:, kb * P:(kb + 1) * P],
                                                ident2[:, :], start=True, stop=True)
                    last.then_inc(p0_full, 1)
                    n_p0 += 1
                elif kind == "Q":
                    p0_ready()
                    seg, j = key
                    at = (seg % SEGMENTS // 2 * PAIRS + j) * P
                    three_passes(p0_bank, lambda a, c: (wqk_hi, wqk_lo)[a][:, c, at:at + P],
                                 lambda b, c: x_blocks((xT_hi, xT_lo)[b], c, seg)
                                 ).then_inc(p0_full, 1)
                    n_p0 += 1
                if kind == "MAX":
                    n_max_of[key[0]] = n_max

        n_max_of = {}

        def count_joined(plan, unit):
            units = [key for kind, key in plan if kind == "MT" and block_of(key) >= 4]
            return units.index(unit) + 1

        def scalar_program(act, plan):
            count = Count(plan)
            n_p0 = 0

            def segment_left(seg):
                if seg >= 2:
                    act.wait_ge(st_full, 2 * (seg - 1) * SEG_STEPS)

            for kind, key in plan:
                if kind == "ST":
                    t, unit, s = key
                    old = t - PT_SLOTS
                    for g in range(2):
                        act.wait_ge(st_full, 2 * t + g + 1)
                        if g == 0 and old >= 0:
                            act.wait_ge(pv_done, old + 1)
                            old_unit = max(u for u in range(unit + 1) if first_step(u) <= old)
                            diagonal = first_step(old_unit) == old
                            if diagonal and block_of(old_unit) == 0:
                                act.wait_ge(p1_full, count.p1("R", old_unit) + 1)
                            elif diagonal:
                                act.wait_ge(pool_done, 2 * old + 4)
                            else:
                                act.wait_ge(pool_done, 2 * old + 2)
                        nc.scalar.activation(probs[:, t % PT_SLOTS, g * BANK:(g + 1) * BANK],
                                             st_bank[(2 * t + g) % ST_BANKS],
                                             ACT.Exp).then_inc(exp_done, 1)
                elif kind == "PV" and key[2] == block_of(key[1]):
                    t, unit, s = key
                    act.wait_ge(pv_done, t + 1)
                    if unit >= Y_SLOTS:
                        act.wait_ge(y_normal, unit - Y_SLOTS + 1)
                    nc.scalar.activation(y[:, unit % Y_SLOTS, :], y_bank, ACT.Copy).then_inc(y_copied, 1)
                elif kind == "MT":
                    act.wait_ge(p1_full, count.p1(kind, key) + 1)
                    n = count.of(kind, key)
                    if n >= 4:
                        act.wait_ge(row_placed[n % 4], 16 * (n // 4))
                    nc.scalar.activation(neg_rows[:, n % 4, :], p1_bank[0:OCTET, 0:P], ACT.Copy,
                                         scale=-1.0).then_inc(p1_free, 1)
                elif kind == "R":
                    act.wait_ge(p1_full, count.p1(kind, key) + 1)
                    if key >= Y_SLOTS:
                        act.wait_ge(p1_full, count.p1("O", key - Y_SLOTS) + 1)
                    nc.scalar.activation(norm[:, key % Y_SLOTS, :], p1_bank,
                                         ACT.Copy).then_inc(p1_free, 1)
                elif kind == "FA":
                    n = count.of("F", key)
                    act.wait_ge(p1_free, count.p1("F", key) + 1)
                    nc.scalar.activation(ff[:, 2 + n % 2, :], ff[:, n % 2, :],
                                         ACT.Tanh).then_inc(tanh_done, 1)
                elif kind == "LN2":
                    act.wait_ge(var_ready, count.of("LN1", key) + 1)
                    nc.scalar.activation(ln[:, 1, :], ln[:, 0, :], ACT.Sqrt).then_inc(sqrt_done, 1)
                elif kind in P0_ITEMS:
                    act.wait_ge(p0_full, count.p0(kind, key) + 1)
                    if kind == "T":
                        b, c, half = key
                        nc.scalar.activation(xT_hi[:, c, half * HALF:(half + 1) * HALF], p0_bank,
                                             ACT.Copy).then_inc(p0_hi, 2)
                    elif kind == "K":
                        par, tok = key[0] % 2, slice(key[1] * HALF, (key[1] + 1) * HALF)
                        nc.scalar.activation(k_hilo[par][:, tok], p0_bank,
                                             ACT.Copy).then_inc(p0_hi, 1)
                        nc.scalar.activation(k_ones[par][0:LATENT, tok], p0_bank[0:LATENT, :],
                                             ACT.Copy).then_inc(p0_hi, 1)
                    elif kind == "KN":
                        nc.scalar.activation(
                            latent[key % 2][:, :, :].rearrange("p b n -> p (b n)"), p0_bank,
                            ACT.Copy).then_inc(p0_hi, 2)
                    elif kind == "Q":
                        seg, j = key
                        segment_left(seg)
                        for g in range(2):
                            rows = slice(g * LATENT, (g + 1) * LATENT)
                            nc.scalar.activation(q_hi[seg % 2][rows, 2 * j + g, :],
                                                 p0_bank[rows, :], ACT.Copy).then_inc(p0_hi, 1)
                    n_p0 += 1

        def vector_program(dve, plan):
            count = Count(plan)
            n_max = n_chain = 0

            def chained(ins):
                nonlocal n_chain
                n_chain += 1
                ins.then_inc(ln_chain, 1)
                dve.wait_ge(ln_chain, n_chain)

            for kind, key in plan:
                if kind == "MAX":
                    unit, h, k0, w = key
                    dve.wait_ge(max_full, n_max + 1)
                    bank = max_bank[n_max % 2][:, 0:w]
                    if h == 0 and k0 == 0 and count.has("MT", unit - 4):
                        dve.wait_ge(p1_full, count.p1("MT", unit - 4) + 1)
                    if k0 + w == (block_of(unit) + 1) * P:
                        nc.vector.tensor_tensor_reduce(
                            bank, bank, causal[:, L - w:L], 1.0, LOWEST, ALU.add,
                            ALU.max, maxima[:, unit % 4, h:h + 1]).then_inc(max_free, 1)
                        ends = h == OCTET - 1
                    else:
                        nc.vector.tensor_reduce(maxima0[:, unit % 4, h:h + 1], bank, AX.X,
                                                ALU.max).then_inc(max_free, 1)
                        ends = False
                    n_max += 1
                    if ends and k0 > 0:
                        dve.wait_ge(max_free, n_max)
                        nc.vector.tensor_tensor(maxima[:, unit % 4, :], maxima[:, unit % 4, :],
                                                maxima0[:, unit % 4, :],
                                                ALU.max).then_inc(max_joined, 1)
                elif kind == "RC":
                    unit, k = key
                    slot = unit % Y_SLOTS
                    if k == 0:
                        dve.wait_ge(p1_free, count.p1("R", unit) + 1)
                    part = norm[:, slot, k * P:(k + 1) * P]
                    nc.vector.reciprocal(part, part).then_inc(recip_done, 1)
                    if k == 3:
                        dve.wait_ge(recip_done, count.of(kind, key) + 1)
                        dve.wait_ge(y_copied, unit + 1)
                        nc.vector.tensor_tensor(norm[:, slot, :], y[:, slot, :], norm[:, slot, :],
                                                ALU.mult).then_inc(y_normal, 1)
                elif kind == "O":
                    i = block_of(key)
                    dve.wait_ge(p1_full, count.p1(kind, key) + 1)
                    if octet_of(key) == 0:
                        dve.wait_ge(ff_added, count.of("FA", (key // UNITS, i)) + 1)
                    else:
                        dve.wait_ge(p1_free, count.p1("O", key - OCTET) + 1)
                    nc.vector.tensor_tensor(acc[:, i, :], acc[:, i, :], p1_bank[:, 0:D],
                                            ALU.add).then_inc(p1_free, 1)
                elif kind == "F":
                    n = count.of("F", key)
                    dve.wait_ge(p1_full, count.p1(kind, key) + 1)
                    if n >= 2:
                        dve.wait_ge(tanh_done, n - 1)
                    nc.vector.tensor_tensor(ff[:, n % 2, :], bias_all[:, :], p1_bank[:, 0:D],
                                            ALU.add).then_inc(p1_free, 1)
                elif kind == "FA":
                    b, i = key
                    n = count.of("FA", key)
                    dve.wait_ge(tanh_done, n + 1)
                    if b > 0:
                        dve.wait_ge(stored[segment_kind(i)], 16 * b * BLOCKS // 2)
                    nc.vector.tensor_tensor(acc[:, i, :], x_in[:, i, :], ff[:, 2 + n % 2, :],
                                            ALU.add).then_inc(ff_added, 1)
                elif kind == "LN1":
                    if key > 0:
                        dve.wait_ge(x_loaded, 16 * (count.of("LN1", key) + 1))
                    for i in range(BLOCKS):
                        last = nc.vector.bn_stats(stats[:, i, :], x_in[:, i, :])
                    chained(last)
                    for i in range(BLOCKS):
                        last = nc.vector.bn_aggr(mean_var[:, i, :], stats[:, i, :])
                    chained(last)
                    nc.vector.tensor_scalar(ln[:, 0, :], mean_var[:, :, 1], EPS, None,
                                            ALU.add).then_inc(var_ready, 1)
                elif kind == "LN3":
                    dve.wait_ge(sqrt_done, count.of("LN2", key) + 1)
                    chained(nc.vector.reciprocal(ln[:, 2, :], ln[:, 1, :]))
                    chained(nc.vector.tensor_tensor(ln[:, 3, :], ln[:, 2, :], ln[:, 2, :],
                                                    ALU.mult))
                    chained(nc.vector.tensor_tensor(ln[:, 4, :], ln[:, 3, :], ln[:, 0, :],
                                                    ALU.mult))
                    chained(nc.vector.tensor_scalar(ln[:, 3, :], ln[:, 4, :], -0.5, 1.5, ALU.mult,
                                                    ALU.add))
                    chained(nc.vector.tensor_tensor(ln[:, 1, :], ln[:, 2, :], ln[:, 3, :],
                                                    ALU.mult))
                    for i in range(BLOCKS):
                        last = nc.vector.tensor_scalar(xn[:, i, :], x_in[:, i, :],
                                                       mean_var[:, i, 0:1], ln[:, 1, i:i + 1],
                                                       ALU.subtract, ALU.mult)
                    last.then_inc(xn_ready, 1)
                elif kind in P0_ITEMS:
                    n = count.p0(kind, key)
                    dve.wait_ge(p0_hi, 2 * n + 2)
                    if kind == "T":
                        b, c, half = key
                        tok = slice(half * HALF, (half + 1) * HALF)
                        nc.vector.tensor_tensor(xT_lo[:, c, tok], p0_bank,
                                                xT_hi[:, c, tok].bitcast(F32),
                                                ALU.subtract).then_inc(p0_free, 1)
                    elif kind == "K":
                        par, tok = key[0] % 2, slice(key[1] * HALF, (key[1] + 1) * HALF)
                        nc.vector.tensor_tensor(k_hilo[par][LATENT:P, tok], p0_bank[LATENT:P, :],
                                                k_hilo[par][LATENT:P, tok].bitcast(F32),
                                                ALU.subtract).then_inc(p0_free, 1)
                    elif kind == "KN":
                        dve.sem_inc(p0_free, 1)
                    elif kind == "Q":
                        seg, j = key
                        for g in range(2):
                            rows = slice(g * LATENT, (g + 1) * LATENT)
                            last = nc.vector.tensor_tensor(
                                q_lo[seg % 2][0:LATENT, 2 * j + g, :], p0_bank[rows, :],
                                q_hi[seg % 2][rows, 2 * j + g, :].bitcast(F32), ALU.subtract)
                        last.then_inc(p0_free, 1)

        def gpsimd_program(pool, plan):
            count = Count(plan)
            for kind, key in plan:
                if kind != "ST":
                    continue
                t, unit, s = key
                slot = t % PT_SLOTS
                for g in range(2):
                    part = slice(g * BANK, (g + 1) * BANK)
                    pool.wait_ge(exp_done, 2 * t + g + 1)
                    if s == 0:
                        v = probs[:, slot, part].rearrange("p (h q) -> p h q", q=P)
                        nc.gpsimd.affine_select(
                            out=v, in_=v, pattern=[[0, 4], [1, P]], compare_op=ALU.is_ge, fill=0.0,
                            base=0, channel_multiplier=-1).then_inc(pool_done, 1)
                        continue
                    if s == 1:
                        if unit >= 2:
                            pool.wait_ge(p1_full, count.p1("R", unit - 2) + 1)
                        other = probs[:, (t - 1) % PT_SLOTS, part]
                    else:
                        other = p_sum[:, unit % 2, part]
                    pool.wait_ge(pool_done, 2 * t + g - 1)
                    nc.gpsimd.tensor_tensor(p_sum[:, unit % 2, part], other, probs[:, slot, part],
                                            ALU.add).then_inc(pool_done, 1)

        x_by_turn = x.rearrange("(t n) l d -> t n l d", n=IN_BODY)
        out_by_turn = out.rearrange("(t n) l d -> t n l d", n=IN_BODY)

        def sync_program(sp, plan, turn):
            count = Count(plan)
            for kind, key in plan:
                if kind == "Q":
                    seg, j = key
                    sp.wait_ge(p0_hi, 2 * count.p0(kind, key) + 2)
                    top, low = slice(0, LATENT), slice(LATENT, P)
                    buf = q_hi[seg % 2]
                    sp.dma_start(buf[low, 2 * j, :].bitcast(F32),
                                 buf[top, 2 * j, :].bitcast(F32)).then_inc(q_twice[j], 16)
                    sp.dma_start(buf[top, 2 * j + 1, :].bitcast(F32),
                                 buf[low, 2 * j + 1, :].bitcast(F32)).then_inc(q_twice[j], 16)
                elif kind == "MT":
                    n = count.of(kind, key)
                    sp.wait_ge(p1_free, count.p1(kind, key) + 1)
                    row = q_lo[key // 4 % 2][LATENT:LATENT + 1, :, columns(key)]
                    sp.dma_start(row.bitcast(F32),
                                 neg_rows[:, n % 4, :].bitcast(F32)).then_inc(row_placed[n % 4], 16)
                elif kind == "O" and octet_of(key) == 1:
                    i = block_of(key)
                    sp.wait_ge(p1_free, count.p1(kind, key) + 1)
                    sp.dma_start(out_by_turn[turn, key // UNITS, i * P:(i + 1) * P, :],
                                 acc[:, i, :]).then_inc(stored[segment_kind(i)], 16)
                elif kind == "LN1" and key > 0:
                    sp.wait_ge(ff_added, BLOCKS * key)
                    at = (turn + key // IN_BODY) % (B // IN_BODY) if key >= IN_BODY else turn
                    nxt = x_by_turn[at, key % IN_BODY]
                    sp.dma_start(x_in[:, :, :], nxt.rearrange("(i p) d -> p i d", p=P)
                                 ).then_inc(x_loaded, 16)
            for j in range(PAIRS):
                sp.wait_ge(q_twice[j], 32 * sum(k == "Q" and key[1] == j for k, key in plan))
            turned = sum(k == "MT" for k, _ in plan)
            for i in range(min(4, turned)):
                sp.wait_ge(row_placed[i], 16 * ((turned - i + 3) // 4))
            outputs = sum(k == "O" and octet_of(u) == 1 for k, u in plan)
            if outputs:
                for s in range(2):
                    sp.wait_ge(stored[s], 16 * outputs // 2)

        def run(plan, turn):
            with nc.Block() as block:
                @block.tensor
                def _(pe):
                    tensor_program(pe, plan)

                @block.scalar
                def _(act):
                    scalar_program(act, plan)

                @block.vector
                def _(dve):
                    vector_program(dve, plan)

                @block.gpsimd
                def _(pool):
                    gpsimd_program(pool, plan)

                @block.sync
                def _(sp):
                    sync_program(sp, plan, turn)

            nc.all_engine_barrier(sems_to_clear=range(names[0].num, names[-1].num + 1))

        run(first_plan(), 0)
        plan = body_plan(IN_BODY)
        with nc.Fori(0, B // IN_BODY) as turn:
            run(plan, turn)


_INS = ["L0_attn_x_bld", "L0_attn_Wq", "L0_attn_Wkv_down", "L0_attn_Wk_up", "L0_attn_Wv_up",
        "L0_attn_Wout", "L0_ffn_weight", "L0_ffn_aux_weight1", "L0_ffn_aux_weight2", "L0_ffn_bias"]


def kernel(**inputs):
    import numpy as np
    import concourse.bacc as bacc
    from concourse.bass_utils import run_bass_kernel_spmd

    nc = bacc.Bacc("TRN2", target_bir_lowering=False, num_devices=1)
    arrays, args = {}, []
    for name in _INS:
        a = np.ascontiguousarray(inputs[name])
        arrays[f"in_{name}"] = a
        args.append(nc.dram_tensor(f"in_{name}", a.shape, F32, kind="ExternalInput").ap())
    shape = arrays["in_L0_attn_x_bld"].shape
    args.append(nc.dram_tensor("out_x", shape, F32, kind="ExternalOutput").ap())
    build(nc, *args)
    result = run_bass_kernel_spmd(nc, [arrays], core_ids=[0])
    return result.results[0]["out_x"]
```

```python
from contextlib import ExitStack

import concourse.bass as bass
from concourse import mybir

ALU = mybir.AluOpType
ACT = mybir.ActivationFunctionType
AX = mybir.AxisListType
F32 = mybir.dt.float32
F32R = mybir.dt.float32r

P = 128
BANK = 512
LATENT = 64
HEADS, HD = 16, 64
OCTET = 8
OCTETS = HEADS // OCTET
PAIRS = OCTET // 2
MAX_BANKS = 3
LOWEST = -3.0e38
EPS = 1e-5

SEGMENT_BLOCKS = [[3, 7, 4, 0], [5, 6, 2, 1]]
PLACE = {0: 0, 3: 1, 4: 2, 7: 3, 1: 0, 2: 1, 5: 2, 6: 3}
BLOCKS = 8
SEGMENTS = 2 * OCTETS
UNITS = 4 * SEGMENTS
STEPS = OCTETS * BLOCKS * (BLOCKS + 1) // 2
SEG_STEPS = STEPS // SEGMENTS
AHEAD = 2
LAG = 2
ST_BANKS, PT_SLOTS, Y_SLOTS, SUM_SLOTS = 2, 4, 3, 3


def block_of(unit):
    return SEGMENT_BLOCKS[unit // 4 % 2][unit % 4]


def segment_kind(block):
    return 0 if block in SEGMENT_BLOCKS[0] else 1


def octet_of(unit):
    return unit % UNITS // OCTET


def first_step(unit):
    n, r = divmod(unit, UNITS)
    return n * STEPS + sum(block_of(u) + 1 for u in range(r))


def key_block(unit, s):
    return block_of(unit) if s == 0 else s - 1


def max_chunks(unit):
    keys = (block_of(unit) + 1) * P
    cuts = [(0, min(keys, BANK))] + ([(BANK, keys - BANK)] if keys > BANK else [])
    return [(unit, h, k0, w) for h in range(OCTET) for k0, w in cuts]


OFF_PE = ("X", "QL", "TL", "KL", "FT", "FA", "RC", "LN1", "LN2", "LN3")


def two_parts(kind, key):
    return [(kind + "0", key), (kind, key)]


def body_plan(batches):
    n_steps = batches * STEPS
    slots = [[] for _ in range(n_steps + 14)]
    due = [[] for _ in slots]
    first = [[] for _ in slots]
    for b in range(batches):
        for s in range(SEGMENTS):
            at = b * STEPS + s * SEG_STEPS
            for j, k in enumerate((0, 2, 3, 5)):
                due[at + k] += two_parts("Q", (b * SEGMENTS + s + 1, j))
                first[at + k + 1].append(("QL", (b * SEGMENTS + s + 1, j)))
            if s < 2:
                for k, i in enumerate(SEGMENT_BLOCKS[s]):
                    due[at + 2 * k + 1].append(("F", (b, i)))
                    due[at + 2 * k + 2].append(("FT", (b, i)))
                    due[at + 2 * k + 3].append(("FA", (b, i)))
        at = b * STEPS + 2 * SEG_STEPS
        due[at - 8].append(("X", b + 1))
        due[at + 1].append(("LN1", b + 1))
        due[at + 3].append(("LN2", b + 1))
        due[at + 5].append(("LN3", b + 1))
        for k in range(4):
            due[at + 8 + k].append(("T", (b + 1, k // 2, k % 2)))
            first[at + 9 + k].append(("TL", (b + 1, k // 2, k % 2)))
        for k in range(2):
            due[at + 13 + k] += two_parts("K", (b + 1, k))
            first[at + 14 + k].append(("KL", (b + 1, k)))
        due[at + 16].append(("KN", b + 1))
    for u in range(batches * UNITS):
        last = first_step(u) + block_of(u)
        due[last + (3 if block_of(u) == 0 else 6)].append(("R", u))
        for k in range(4):
            due[last + 7 + k].append(("RC", (u, k)))
        due[last + 13].append(("O", u))
    stream = [c for u in range(AHEAD, batches * UNITS + AHEAD) for c in max_chunks(u)]
    sent = n = 0
    step_of = [(u, s) for u in range(batches * UNITS) for s in range(block_of(u) + 1)]
    for t, slot in enumerate(slots):
        chunks, turns = [], []
        while n < len(stream) and sent < OCTET * P * (t + 1):
            chunks.append(("MAX", stream[n]))
            sent += stream[n][3]
            n += 1
            if n == len(stream) or stream[n][0] != stream[n - 1][0]:
                turns.append(("MT", stream[n - 1][0]))
        for item in turns:
            due[t + 2].insert(0, item)
        p1 = [item for item in due[t] if item[0] in ("MT", "R", "F", "O")]
        p1 = [two_parts(*item) if item[0] == "O" else [item] for item in p1] + [[], [], []]
        others = [item for item in due[t] if item[0] not in ("MT", "R", "F", "O")]
        st = [[("ST", (t, *step_of[t], g))] if t < n_steps else [] for g in range(2)]
        pv = [("PV", (t - LAG, *step_of[t - LAG]))] if LAG <= t < n_steps + LAG else []
        work = first[t] + st[0] + p1[0] + st[1] + others + p1[1] + pv + sum(p1[2:], [])
        n_chunks = len(chunks)
        on_pe = [k for k, item in enumerate(work) if item[0] not in OFF_PE]
        for k, item in enumerate(work):
            slot.append(item)
            if k in on_pe:
                done = on_pe.index(k) + 1
                while len(chunks) > (len(on_pe) - done) * n_chunks / len(on_pe):
                    slot.append(chunks.pop(0))
        slot += chunks
    return [item for slot in slots for item in slot]


def first_plan():
    plan = [("LN1", 0), ("LN2", 0), ("W", "constants"), ("LN3", 0), ("W", "turn wq"),
            ("T", (0, 0, 0)), ("W", "fold wqk")]
    for k in range(4):
        plan += [("T", (0, k // 2, k % 2))] * (k > 0) + [("TL", (0, k // 2, k % 2))]
    for k in range(2):
        plan += two_parts("K", (0, k)) + [("KL", (0, k))]
    plan.append(("KN", 0))
    for j in range(PAIRS):
        plan += two_parts("Q", (0, j)) + [("QL", (0, j))]
    maxima = [[("MAX", c) for c in max_chunks(u)] for u in range(AHEAD)]
    return (plan + [("W", "turn others")] + maxima[0] + [("W", "fold wvo"), ("MT", 0)] + maxima[1]
            + [("W", "fold wff"), ("MT", 1)])


P0_ITEMS = ("T", "K", "KN", "Q")
P1_ITEMS = ("MT", "R", "O", "F")


class Count:

    def __init__(self, plan):
        self.at = {}
        n = {}
        for kind, key in plan:
            group = "P0" if kind in P0_ITEMS else "P1" if kind in P1_ITEMS else kind
            for name in {group, kind}:
                self.at[name, kind, key] = n.get(name, 0)
                n[name] = n.get(name, 0) + 1

    def has(self, kind, key):
        return (kind, kind, key) in self.at

    def of(self, kind, key):
        return self.at[kind, kind, key]

    def p0(self, kind, key):
        return self.at["P0", kind, key]

    def p1(self, kind, key):
        return self.at["P1", kind, key]


def build(nc, x, Wq, Wkv_down, Wk_up, Wv_up, Wout, weight, aux1, aux2, bias, out):
    B, L, D = x.shape
    C = D // P
    IN_BODY = 2
    HALF = 4 * P
    assert L == BLOCKS * P and D == 256 and B % IN_BODY == 0

    ctx = ExitStack()
    with ctx:
        def sb(name, shape, dt=F32):
            return ctx.enter_context(nc.sbuf_tensor(name, shape, dt))

        names = []

        def sem(name):
            names.append(ctx.enter_context(nc.semaphore(name)))
            return names[-1]

        q_hi = [sb(f"q_hi{i}", [P, OCTET, HALF], F32R) for i in range(2)]
        q_lo = [sb(f"q_lo{i}", [LATENT + 1, OCTET, HALF], F32R) for i in range(2)]
        k_hilo = [sb(f"k_hilo{i}", [P, L], F32R) for i in range(2)]
        k_ones = [sb(f"k_ones{i}", [LATENT + 1, L], F32R) for i in range(2)]
        latent = [sb(f"latent{i}", [P, BLOCKS, LATENT]) for i in range(2)]
        probs = sb("probs", [P, PT_SLOTS, 2 * BANK])
        p_sum = sb("p_sum", [P, SUM_SLOTS, 2 * BANK])
        x_in = sb("x_in", [P, BLOCKS, D])
        xn = sb("xn", [P, BLOCKS, D])
        acc = sb("acc", [P, BLOCKS, D])
        xT_hi = sb("xT_hi", [P, C, L], F32R)
        xT_lo = sb("xT_lo", [P, C, L], F32R)
        y = sb("y", [P, Y_SLOTS, BANK])
        norm = sb("norm", [P, Y_SLOTS, BANK])
        wqk_hi = sb("wqk_hi", [P, C, HEADS * LATENT], F32R)
        wqk_lo = sb("wqk_lo", [P, C, HEADS * LATENT], F32R)
        wvo = sb("wvo", [P, HEADS // 2, D])
        wff_hi = sb("wff_hi", [P, C, D], F32R)
        wff_lo = sb("wff_lo", [P, C, D], F32R)
        wkv_hi = sb("wkv_hi", [P, C, 2 * LATENT], F32R)
        wkv_lo = sb("wkv_lo", [P, C, 2 * LATENT], F32R)
        bias_all = sb("bias_all", [P, D])
        ident = sb("ident", [P, P])
        ident_f = sb("ident_f", [P, LATENT])
        ident2 = sb("ident2", [P, LATENT], F32R)
        ones = sb("ones", [P, LATENT])
        causal = sb("causal", [P, L])
        maxima = sb("maxima", [P, 4, OCTET])
        maxima0 = sb("maxima0", [P, 4, OCTET])
        neg_rows = sb("neg_rows", [OCTET, 4, P], F32R)
        ff = sb("ff", [P, 4, D])
        stats = sb("stats", [P, BLOCKS, 6])
        mean_var = sb("mean_var", [P, BLOCKS, 2])
        ln = sb("ln", [P, 5, BLOCKS])

        ps = ctx.enter_context(nc.psum_tensor("ps", [P, 8, BANK], F32))
        st_bank = [ps[:, i, :] for i in range(ST_BANKS)]
        max_bank = [ps[:, ST_BANKS + i, :] for i in range(MAX_BANKS)]
        y_bank, p1_bank = ps[:, 5, :], ps[:, 7, :]
        wq_banks = [ps[:, n, :] for n in (2, 3, 4, 7)]
        wk_bank = ps[:, 5, :]

        wkv_loaded = sem("wkv_loaded")
        wqk_loaded = sem("wqk_loaded")
        others_loaded = sem("others_loaded")
        consts_made = sem("consts_made")
        w_full = sem("w_full")
        w_copied = sem("w_copied")
        w_split = sem("w_split")
        x_loaded = sem("x_loaded")
        ln_chain = sem("ln_chain")
        var_ready = sem("var_ready")
        sqrt_done = sem("sqrt_done")
        xn_ready = sem("xn_ready")
        p0_full = sem("p0_full")
        p0_hi = sem("p0_hi")
        p0_free = sem("p0_free")
        q_twice = [sem(f"q_twice{j}") for j in range(PAIRS)]
        max_full = sem("max_full")
        max_free = sem("max_free")
        max_joined = sem("max_joined")
        row_ready = sem("row_ready")
        row_placed = [sem(f"row_placed{i}") for i in range(4)]
        st_full = sem("st_full")
        exp_done = sem("exp_done")
        pool_done = sem("pool_done")
        pv_done = sem("pv_done")
        y_copied = sem("y_copied")
        p1_full = sem("p1_full")
        p1_free = sem("p1_free")
        recip_done = sem("recip_done")
        y_normal = sem("y_normal")
        tanh_done = sem("tanh_done")
        ff_added = sem("ff_added")
        stored = [sem(f"stored{s}") for s in range(2)]

        wq_in = probs[:, 0:2, :].rearrange("p a n -> p (a n)").rearrange("p (c n) -> p c n", c=C)
        wqT = probs[:, 2:4, :].rearrange("p a n -> p (a n)").rearrange("p (j d) -> p j d", d=D)
        wk_in, wv_in = p_sum[0:LATENT, 0, :], p_sum[0:LATENT, 1, :]
        acc_flat = acc[:, :, :].rearrange("p a n -> p (a n)")
        wkT = acc_flat[:, 0:512].rearrange("p (j n) -> p j n", n=LATENT)
        wvT = acc_flat[:, 512:1024].rearrange("p (j n) -> p j n", n=LATENT)
        aux12 = acc_flat[:, 1024:1536].rearrange("p (c n) -> p c n", c=C)
        wT = acc_flat[:, 1536:2048].rearrange("p (c n) -> p c n", c=C)
        wout_in = xn[:, :, :]
        w_in = y[:, 0, :].rearrange("p (c n) -> p c n", c=C)
        aux1_in = y[:, 1, :].rearrange("p (c n) -> p c n", c=C)
        aux2_in = y[:, 2, :].rearrange("p (c n) -> p c n", c=C)
        aux1T = norm[:, 0, :].rearrange("p (c n) -> p c n", c=C)
        wkv_in = norm[:, 1, 0:C * LATENT].rearrange("p (c n) -> p c n", c=C)

        def x_blocks(xT, c, seg):
            v = xT[:, c, :].rearrange("p (a b q) -> p a b q", a=2, b=4)
            return v[:, :, 0:4:3, :] if seg % 2 == 0 else v[:, :, 1:3, :]

        def columns(unit):
            return slice(PLACE[block_of(unit)] * P, (PLACE[block_of(unit)] + 1) * P)

        def load_all(sp):
            for dst, src, signal in (
                (x_in[:, :, :], x[0].rearrange("(i p) d -> p i d", p=P), x_loaded),
                (wkv_in, Wkv_down.rearrange("(c p) n -> p c n", p=P), wkv_loaded),
                (wq_in, Wq.rearrange("(c p) h k -> p c (h k)", p=P), wqk_loaded),
                (wk_in, Wk_up.rearrange("c h k -> c (h k)"), wqk_loaded),
                (wv_in, Wv_up.rearrange("c h k -> c (h k)"), others_loaded),
                (aux1_in, aux1.rearrange("(c p) n -> p c n", p=P), others_loaded),
                (w_in, weight.rearrange("(c p) n -> p c n", p=P), others_loaded),
                (aux2_in, aux2.rearrange("(c p) n -> p c n", p=P), others_loaded),
                (bias_all[:, :], bias.rearrange("(a n) -> a n", a=1).broadcast_to([P, D]),
                 others_loaded),
                (wout_in, Wout.rearrange("(j a) k o -> (a k) j o", a=2), others_loaded),
            ):
                if dst is wout_in:
                    sp.wait_ge(p0_full, 4)
                sp.dma_start(dst, src).then_inc(signal, 16)

        def make_constants(pool):
            nc.gpsimd.memset(ident[:, :], 0.0).then_inc(consts_made, 1)
            nc.gpsimd.memset(ident_f[:, :], 0.0).then_inc(consts_made, 1)
            nc.gpsimd.memset(causal[:, :], 0.0).then_inc(consts_made, 1)
            pool.wait_ge(consts_made, 3)
            nc.gpsimd.affine_select(
                out=ident[:, :], in_=ident[:, :], pattern=[[-1, P]], compare_op=ALU.not_equal,
                fill=1.0, base=0, channel_multiplier=1).then_inc(consts_made, 1)
            nc.gpsimd.affine_select(
                out=ident_f[:, :], in_=ident_f[:, :], pattern=[[-1, LATENT]],
                compare_op=ALU.not_equal, fill=1.0, base=0, channel_multiplier=1,
            ).then_inc(consts_made, 1)
            pool.wait_ge(consts_made, 5)
            nc.gpsimd.affine_select(
                out=ident_f[:, :], in_=ident_f[:, :], pattern=[[-1, LATENT]],
                compare_op=ALU.not_equal, fill=1.0, base=-LATENT, channel_multiplier=1,
            ).then_inc(consts_made, 1)
            nc.gpsimd.affine_select(
                out=causal[:, L - P:L], in_=causal[:, L - P:L], pattern=[[-1, P]],
                compare_op=ALU.is_ge, fill=LOWEST, base=0, channel_multiplier=1,
            ).then_inc(consts_made, 1)

        def fold_on_pe(pe, what, p0_uses):
            def square(bank, left, right):
                for c in range(C):
                    for k in range(C):
                        last = nc.tensor.matmul(ps[:, bank, c * D:(c + 1) * D],
                                                left[:, k, c * P:(c + 1) * P], right[:, k, :],
                                                start=(k == 0), stop=(k == C - 1))
                last.then_inc(w_full, 1)

            def wvo_bank(bank, n):
                for h in range(4 * n, 4 * n + 4):
                    r, at = (h % 2) * HD, (h // 2 % 2) * D
                    last = nc.tensor.matmul(ps[r:r + LATENT, bank, at:at + D],
                                            wvT[r:r + HD, h // 2, :], wout_in[r:r + HD, h // 2, :],
                                            start=True, stop=True)
                last.then_inc(w_full, 1)

            def transposes(dst, pieces):
                for n, piece in enumerate(pieces):
                    rows = piece.shape[0]
                    last = nc.tensor.transpose(dst[:, n * rows:(n + 1) * rows], piece,
                                               ident[0:rows, 0:rows])
                last.then_inc(w_full, 1)

            if what == "constants":
                pe.wait_ge(consts_made, 7)
                pe.wait_ge(w_split, CONSTANTS)
            elif what == "turn wq":
                pe.wait_ge(wqk_loaded, 32)
                for n in range(4):
                    transposes(wq_banks[n], [wq_in[:, c, j * P:(j + 1) * P]
                                             for j in (2 * n, 2 * n + 1) for c in range(C)])
                transposes(wk_bank, [wk_in[:, j * P:(j + 1) * P] for j in range(HEADS // 2)])
            elif what == "fold wqk":
                pe.wait_ge(w_copied, 5)
                for c in range(C):
                    for g in range(2):
                        r = g * HD
                        for j in range(HEADS // 2):
                            last = nc.tensor.matmul(
                                wq_banks[2 * c + g][:, j * LATENT:(j + 1) * LATENT],
                                wqT[r:r + HD, j, c * P:(c + 1) * P], wkT[r:r + HD, j, :],
                                start=True, stop=True)
                        last.then_inc(w_full, 1)
            elif what == "turn others":
                pe.wait_ge(p0_free, p0_uses)
                pe.wait_ge(others_loaded, 96)
                transposes(ps[:, 5, :], [wv_in[:, j * P:(j + 1) * P] for j in range(HEADS // 2)])
                for bank, w in ((0, aux1_in), (1, w_in)):
                    transposes(ps[:, bank, :], [w[:, c, k * P:(k + 1) * P]
                                                for k in range(C) for c in range(C)])
            elif what == "fold wvo":
                pe.wait_ge(w_copied, 12)
                square(6, aux1T, aux2_in)
                for n, bank in enumerate((5, 0, 1)):
                    wvo_bank(bank, n)
            elif what == "fold wff":
                pe.wait_ge(w_copied, 14)
                square(6, wT, aux12)
                wvo_bank(5, 3)

        def fold_on_act(act, what):
            def copied(n, dst, bank, **scale):
                act.wait_ge(w_full, n)
                nc.scalar.activation(dst, bank, ACT.Copy, **scale).then_inc(w_copied, 1)

            def wvo_part(n):
                return wvo[:, 2 * n:2 * n + 2, :].rearrange("p j d -> p (j d)")

            if what == "turn wq":
                wqT_flat = wqT.rearrange("p j d -> p (j d)")
                for n in range(4):
                    copied(n + 1, wqT_flat[:, n * BANK:(n + 1) * BANK], wq_banks[n])
                copied(5, acc_flat[:, 0:512], wk_bank)
            elif what == "fold wqk":
                for n in range(4):
                    copied(6 + n, *wqk_part(wqk_hi, n), scale=HD ** -0.5)
            elif what == "turn others":
                copied(10, acc_flat[:, 512:1024], ps[:, 5, :])
                copied(11, norm[:, 0, :], ps[:, 0, :])
                copied(12, acc_flat[:, 1536:2048], ps[:, 1, :])
            elif what == "fold wvo":
                copied(13, acc_flat[:, 1024:1536], ps[:, 6, :])
                for n, bank in enumerate((5, 0, 1)):
                    copied(14 + n, wvo_part(n), ps[:, bank, :])
            elif what == "fold wff":
                copied(17, wff_hi[:, :, :].rearrange("p c n -> p (c n)"), ps[:, 6, :])
                copied(18, wvo_part(3), ps[:, 5, :])

        def wqk_part(w, n):
            return (w[:, n // 2, :].rearrange("p (j g n) -> p j g n", g=2, n=LATENT)
                    [:, :, n % 2, :], wq_banks[n].rearrange("p (j n) -> p j n", n=LATENT))

        CONSTANTS = 8

        def fold_on_dve(dve, what):
            if what == "constants":
                dve.wait_ge(wkv_loaded, 16)
                dve.wait_ge(consts_made, 7)
                both = [slice(r * LATENT, (r + 1) * LATENT) for r in range(2)]
                for cols in both:
                    nc.vector.tensor_copy(wkv_hi[:, :, cols], wkv_in).then_inc(w_split, 1)
                nc.vector.tensor_copy(ident2[:, :], ident_f[:, :]).then_inc(w_split, 1)
                nc.vector.memset(ones[:, :], 1.0).then_inc(w_split, 1)
                for i in range(2):
                    nc.vector.tensor_scalar(k_ones[i][LATENT:LATENT + 1, :], causal[64:65, :], 0.0,
                                            1.0, ALU.mult, ALU.add).then_inc(w_split, 1)
                dve.wait_ge(w_split, 2)
                for cols in both:
                    nc.vector.tensor_tensor(wkv_lo[:, :, cols], wkv_in,
                                            wkv_hi[:, :, cols].bitcast(F32),
                                            ALU.subtract).then_inc(w_split, 1)
            elif what == "fold wqk":
                for n in range(4):
                    lo, bank = wqk_part(wqk_lo, n)
                    dve.wait_ge(w_copied, 6 + n)
                    nc.vector.scalar_tensor_tensor(
                        out=lo, in0=bank, scalar=HD ** -0.5,
                        in1=wqk_part(wqk_hi, n)[0].bitcast(F32), op0=ALU.mult,
                        op1=ALU.subtract).then_inc(w_split, 1)
            elif what == "fold wff":
                dve.wait_ge(w_copied, 17)
                nc.vector.tensor_tensor(wff_lo[:, :, :].rearrange("p c n -> p (c n)"), ps[:, 6, :],
                                        wff_hi[:, :, :].rearrange("p c n -> p (c n)").bitcast(F32),
                                        ALU.subtract).then_inc(w_split, 1)

        def tensor_program(pe, plan, p0_banks):
            count = Count(plan)
            n_max = n_p0 = n_p1 = 0

            def three_passes(dst, weights, moving, chunks=range(C)):
                for c in chunks:
                    for n, (a, b) in enumerate(((0, 0), (0, 1), (1, 0))):
                        last = nc.tensor.matmul(dst, weights(a, c), moving(b, c),
                                                start=(c == 0 and n == 0),
                                                stop=(c == C - 1 and n == 2))
                return last

            def p0_ready():
                if n_p0 >= len(p0_banks):
                    pe.wait_ge(p0_free, n_p0 - len(p0_banks) + 1)

            def p1_ready():
                if n_p1:
                    pe.wait_ge(p1_free, n_p1)

            for kind, key in plan:
                p0_bank = p0_banks[n_p0 % len(p0_banks)]
                if kind == "ST":
                    t, unit, s, g = key
                    kb = key_block(unit, s)
                    seg, par = unit // 4 % 2, unit // UNITS % 2
                    blk = slice(kb * P, (kb + 1) * P)
                    if g == 0 and s == 0 and count.has("MT", unit):
                        n = count.of("MT", unit)
                        pe.wait_ge(row_placed[n % 4], 16 * (n // 4 + 1))
                    n = 2 * t + g
                    if n >= ST_BANKS:
                        pe.wait_ge(exp_done, n - ST_BANKS + 1)
                    bank = st_bank[n % ST_BANKS]
                    nc.tensor.matmul(bank, k_hilo[par][:, blk],
                                     q_hi[seg][:, g:OCTET:2, columns(unit)],
                                     start=True, stop=False)
                    nc.tensor.matmul(bank, k_ones[par][:, blk],
                                     q_lo[seg][:, g:OCTET:2, columns(unit)],
                                     start=False, stop=True).then_inc(st_full, 1)
                elif kind == "PV":
                    t, unit, s = key
                    par = unit // UNITS % 2
                    for g in range(2):
                        if s == 0:
                            pe.wait_ge(pool_done, 2 * t + g + 1)
                            if unit > 0:
                                pe.wait_ge(y_copied, unit)
                        else:
                            pe.wait_ge(exp_done, 2 * t + g + 1)
                        last = nc.tensor.matmul(y_bank[g * LATENT:(g + 1) * LATENT, :],
                                                latent[par][:, key_block(unit, s), :],
                                                probs[:, t % PT_SLOTS, g * BANK:(g + 1) * BANK],
                                                start=(s == 0), stop=(s == block_of(unit)))
                    last.then_inc(pv_done, 1)
                elif kind == "MAX":
                    unit, h, k0, w = key
                    seg, par = unit // 4, unit // UNITS % 2
                    if n_max >= MAX_BANKS:
                        pe.wait_ge(max_free, n_max - MAX_BANKS + 1)
                    if count.has("Q", (seg, h // 2)):
                        n = count.of("Q", (seg, h // 2))
                        pe.wait_ge(q_twice[h // 2], 32 * (n // PAIRS + 1))
                    nc.tensor.matmul(max_bank[n_max % MAX_BANKS][:, 0:w], q_hi[seg % 2][:, h, columns(unit)],
                                     k_hilo[par][:, k0:k0 + w], start=True,
                                     stop=True).then_inc(max_full, 1)
                    n_max += 1
                elif kind == "MT":
                    p1_ready()
                    if block_of(key) < 4:
                        pe.wait_ge(max_free, n_max_of[key])
                    else:
                        pe.wait_ge(max_joined, count_joined(plan, key))
                    nc.tensor.transpose(p1_bank[0:OCTET, 0:P], maxima[:, key % 4, :],
                                        ident[:, :]).then_inc(p1_full, 1)
                    n_p1 += 1
                elif kind == "R":
                    p1_ready()
                    last_step = first_step(key) + block_of(key)
                    pe.wait_ge(pool_done, 2 * last_step + 2)
                    for g in range(2):
                        part = slice(g * BANK, (g + 1) * BANK)
                        src = (probs[:, last_step % PT_SLOTS, part] if block_of(key) == 0
                               else p_sum[:, key % SUM_SLOTS, part])
                        last = nc.tensor.matmul(p1_bank[g * LATENT:(g + 1) * LATENT, :], ones[:, :],
                                                src, start=True, stop=True)
                    last.then_inc(p1_full, 1)
                    n_p1 += 1
                elif kind in ("O0", "O"):
                    if kind == "O0":
                        p1_ready()
                        pe.wait_ge(y_normal, key + 1)
                    for j in (0, 1) if kind == "O0" else (2, 3):
                        last = nc.tensor.matmul(p1_bank[:, 0:D], norm[:, key % Y_SLOTS, j * P:(j + 1) * P],
                                                wvo[:, octet_of(key) * PAIRS + j, :],
                                                start=(j == 0), stop=(j == PAIRS - 1))
                    if kind == "O":
                        last.then_inc(p1_full, 1)
                        n_p1 += 1
                elif kind == "F":
                    p1_ready()
                    tok = slice(key[1] * P, (key[1] + 1) * P)
                    three_passes(p1_bank[:, 0:D], lambda a, c: (xT_hi, xT_lo)[a][:, c, tok],
                                 lambda b, c: (wff_hi, wff_lo)[b][:, c, :]).then_inc(p1_full, 1)
                    n_p1 += 1
                elif kind == "T":
                    p0_ready()
                    b, c, half = key
                    pe.wait_ge(xn_ready, count.of("LN3", b) + 1)
                    for k in range(4):
                        last = nc.tensor.transpose(p0_bank[:, k * P:(k + 1) * P],
                                                   xn[:, 4 * half + k, c * P:(c + 1) * P],
                                                   ident[:, :])
                    last.then_inc(p0_full, 1)
                    n_p0 += 1
                elif kind in ("K0", "K"):
                    if kind == "K0":
                        p0_ready()
                        pe.wait_ge(p0_free, count.p0("T", (key[0], 1, 1)) + 1)
                    tok = slice(key[1] * HALF, (key[1] + 1) * HALF)
                    last = three_passes(p0_bank, lambda a, c: (wkv_hi, wkv_lo)[a][:, c, :],
                                        lambda b, c: (xT_hi, xT_lo)[b][:, c, tok],
                                        chunks=[0 if kind == "K0" else 1])
                    if kind == "K":
                        last.then_inc(p0_full, 1)
                        n_p0 += 1
                elif kind == "KN":
                    p0_ready()
                    pe.wait_ge(p0_free, count.p0("K", (key, 1)) + 1)
                    for kb in range(BLOCKS):
                        last = nc.tensor.matmul(p0_bank[:, kb * LATENT:(kb + 1) * LATENT],
                                                k_hilo[key % 2][:, kb * P:(kb + 1) * P],
                                                ident2[:, :], start=True, stop=True)
                    last.then_inc(p0_full, 1)
                    n_p0 += 1
                elif kind == "W":
                    fold_on_pe(pe, key, n_p0)
                elif kind in ("Q0", "Q"):
                    if kind == "Q0":
                        if count.has("W", "fold wqk"):
                            pe.wait_ge(w_split, CONSTANTS + 4)
                        p0_ready()
                    seg, j = key
                    at = (seg % SEGMENTS // 2 * PAIRS + j) * P
                    last = three_passes(p0_bank, lambda a, c: (wqk_hi, wqk_lo)[a][:, c, at:at + P],
                                        lambda b, c: x_blocks((xT_hi, xT_lo)[b], c, seg),
                                        chunks=[0 if kind == "Q0" else 1])
                    if kind == "Q":
                        last.then_inc(p0_full, 1)
                        n_p0 += 1
                if kind == "MAX":
                    n_max_of[key[0]] = n_max

        n_max_of = {}

        def count_joined(plan, unit):
            units = [key for kind, key in plan if kind == "MT" and block_of(key) >= 4]
            return units.index(unit) + 1

        def scalar_program(act, plan, p0_banks):
            count = Count(plan)

            def segment_left(seg):
                if seg >= 2:
                    act.wait_ge(st_full, 2 * (seg - 1) * SEG_STEPS)

            for kind, key in plan:
                if kind == "ST":
                    t, unit, s, g = key
                    old = t - PT_SLOTS
                    act.wait_ge(st_full, 2 * t + g + 1)
                    if g == 0 and old >= 0:
                        act.wait_ge(pv_done, old + 1)
                        old_unit = max(u for u in range(unit + 1) if first_step(u) <= old)
                        diagonal = first_step(old_unit) == old
                        if diagonal and block_of(old_unit) == 0:
                            act.wait_ge(p1_full, count.p1("R", old_unit) + 1)
                        elif diagonal:
                            act.wait_ge(pool_done, 2 * old + 4)
                        else:
                            act.wait_ge(pool_done, 2 * old + 2)
                    nc.scalar.activation(probs[:, t % PT_SLOTS, g * BANK:(g + 1) * BANK],
                                         st_bank[(2 * t + g) % ST_BANKS],
                                         ACT.Exp).then_inc(exp_done, 1)
                elif kind == "PV" and key[2] == block_of(key[1]):
                    t, unit, s = key
                    act.wait_ge(pv_done, t + 1)
                    if unit >= Y_SLOTS:
                        act.wait_ge(y_normal, unit - Y_SLOTS + 1)
                    nc.scalar.activation(y[:, unit % Y_SLOTS, :], y_bank, ACT.Copy).then_inc(y_copied, 1)
                elif kind == "MT":
                    act.wait_ge(p1_full, count.p1(kind, key) + 1)
                    n = count.of(kind, key)
                    if n >= 4:
                        act.wait_ge(row_placed[n % 4], 16 * (n // 4))
                    nc.scalar.activation(neg_rows[:, n % 4, :], p1_bank[0:OCTET, 0:P], ACT.Copy,
                                         scale=-1.0).then_inc(p1_free, 1)
                elif kind == "R":
                    act.wait_ge(p1_full, count.p1(kind, key) + 1)
                    if key >= Y_SLOTS:
                        act.wait_ge(p1_full, count.p1("O", key - Y_SLOTS) + 1)
                    nc.scalar.activation(norm[:, key % Y_SLOTS, :], p1_bank,
                                         ACT.Copy).then_inc(p1_free, 1)
                elif kind == "FT":
                    n = count.of("F", key)
                    act.wait_ge(p1_free, count.p1("F", key) + 1)
                    nc.scalar.activation(ff[:, 2 + n % 2, :], ff[:, n % 2, :],
                                         ACT.Tanh).then_inc(tanh_done, 1)
                elif kind == "W":
                    fold_on_act(act, key)
                elif kind == "LN2":
                    act.wait_ge(var_ready, count.of("LN1", key) + 1)
                    nc.scalar.activation(ln[:, 1, :], ln[:, 0, :], ACT.Sqrt).then_inc(sqrt_done, 1)
                elif kind in P0_ITEMS:
                    act.wait_ge(p0_full, count.p0(kind, key) + 1)
                    p0_bank = p0_banks[count.p0(kind, key) % len(p0_banks)]
                    if kind == "T":
                        b, c, half = key
                        nc.scalar.activation(xT_hi[:, c, half * HALF:(half + 1) * HALF], p0_bank,
                                             ACT.Copy).then_inc(p0_hi, 2)
                    elif kind == "K":
                        par, tok = key[0] % 2, slice(key[1] * HALF, (key[1] + 1) * HALF)
                        nc.scalar.activation(k_hilo[par][:, tok], p0_bank,
                                             ACT.Copy).then_inc(p0_hi, 1)
                        nc.scalar.activation(k_ones[par][0:LATENT, tok], p0_bank[0:LATENT, :],
                                             ACT.Copy).then_inc(p0_hi, 1)
                    elif kind == "KN":
                        nc.scalar.activation(
                            latent[key % 2][:, :, :].rearrange("p b n -> p (b n)"), p0_bank,
                            ACT.Copy).then_inc(p0_hi, 2)
                    elif kind == "Q":
                        seg, j = key
                        segment_left(seg)
                        for g in range(2):
                            rows = slice(g * LATENT, (g + 1) * LATENT)
                            nc.scalar.activation(q_hi[seg % 2][rows, 2 * j + g, :],
                                                 p0_bank[rows, :], ACT.Copy).then_inc(p0_hi, 1)

        def vector_program(dve, plan, p0_banks):
            count = Count(plan)
            n_max = n_chain = 0

            def chained(ins):
                nonlocal n_chain
                n_chain += 1
                ins.then_inc(ln_chain, 1)
                dve.wait_ge(ln_chain, n_chain)

            for kind, key in plan:
                if kind == "MAX":
                    unit, h, k0, w = key
                    dve.wait_ge(max_full, n_max + 1)
                    bank = max_bank[n_max % MAX_BANKS][:, 0:w]
                    if h == 0 and k0 == 0 and count.has("MT", unit - 4):
                        dve.wait_ge(p1_full, count.p1("MT", unit - 4) + 1)
                    if k0 + w == (block_of(unit) + 1) * P:
                        nc.vector.tensor_tensor_reduce(
                            bank, bank, causal[:, L - w:L], 1.0, LOWEST, ALU.add,
                            ALU.max, maxima[:, unit % 4, h:h + 1]).then_inc(max_free, 1)
                        ends = h == OCTET - 1
                    else:
                        nc.vector.tensor_reduce(maxima0[:, unit % 4, h:h + 1], bank, AX.X,
                                                ALU.max).then_inc(max_free, 1)
                        ends = False
                    n_max += 1
                    if ends and k0 > 0:
                        dve.wait_ge(max_free, n_max)
                        nc.vector.tensor_tensor(maxima[:, unit % 4, :], maxima[:, unit % 4, :],
                                                maxima0[:, unit % 4, :],
                                                ALU.max).then_inc(max_joined, 1)
                elif kind == "RC":
                    unit, k = key
                    slot = unit % Y_SLOTS
                    if k == 0:
                        dve.wait_ge(p1_free, count.p1("R", unit) + 1)
                    part = norm[:, slot, k * P:(k + 1) * P]
                    nc.vector.reciprocal(part, part).then_inc(recip_done, 1)
                    if k == 3:
                        dve.wait_ge(recip_done, count.of(kind, key) + 1)
                        dve.wait_ge(y_copied, unit + 1)
                        nc.vector.tensor_tensor(norm[:, slot, :], y[:, slot, :], norm[:, slot, :],
                                                ALU.mult).then_inc(y_normal, 1)
                elif kind == "O":
                    i = block_of(key)
                    dve.wait_ge(p1_full, count.p1(kind, key) + 1)
                    if octet_of(key) == 0:
                        dve.wait_ge(ff_added, count.of("FA", (key // UNITS, i)) + 1)
                    else:
                        dve.wait_ge(p1_free, count.p1("O", key - OCTET) + 1)
                    nc.vector.tensor_tensor(acc[:, i, :], acc[:, i, :], p1_bank[:, 0:D],
                                            ALU.add).then_inc(p1_free, 1)
                elif kind == "F":
                    n = count.of("F", key)
                    dve.wait_ge(p1_full, count.p1(kind, key) + 1)
                    if n >= 2:
                        dve.wait_ge(tanh_done, n - 1)
                    nc.vector.tensor_tensor(ff[:, n % 2, :], bias_all[:, :], p1_bank[:, 0:D],
                                            ALU.add).then_inc(p1_free, 1)
                elif kind == "FA":
                    b, i = key
                    n = count.of("FA", key)
                    dve.wait_ge(tanh_done, n + 1)
                    if b > 0:
                        dve.wait_ge(stored[segment_kind(i)], 16 * b * BLOCKS // 2)
                    nc.vector.tensor_tensor(acc[:, i, :], x_in[:, i, :], ff[:, 2 + n % 2, :],
                                            ALU.add).then_inc(ff_added, 1)
                elif kind == "W":
                    fold_on_dve(dve, key)
                elif kind == "LN1":
                    dve.wait_ge(x_loaded, 16 * (count.of("LN1", key) + 1))
                    for i in range(BLOCKS):
                        last = nc.vector.bn_stats(stats[:, i, :], x_in[:, i, :])
                    chained(last)
                    for i in range(BLOCKS):
                        last = nc.vector.bn_aggr(mean_var[:, i, :], stats[:, i, :])
                    chained(last)
                    nc.vector.tensor_scalar(ln[:, 0, :], mean_var[:, :, 1], EPS, None,
                                            ALU.add).then_inc(var_ready, 1)
                elif kind == "LN3":
                    dve.wait_ge(sqrt_done, count.of("LN2", key) + 1)
                    chained(nc.vector.reciprocal(ln[:, 2, :], ln[:, 1, :]))
                    chained(nc.vector.tensor_tensor(ln[:, 3, :], ln[:, 2, :], ln[:, 2, :],
                                                    ALU.mult))
                    chained(nc.vector.tensor_tensor(ln[:, 4, :], ln[:, 3, :], ln[:, 0, :],
                                                    ALU.mult))
                    chained(nc.vector.tensor_scalar(ln[:, 3, :], ln[:, 4, :], -0.5, 1.5, ALU.mult,
                                                    ALU.add))
                    chained(nc.vector.tensor_tensor(ln[:, 1, :], ln[:, 2, :], ln[:, 3, :],
                                                    ALU.mult))
                    for i in range(BLOCKS):
                        last = nc.vector.tensor_scalar(xn[:, i, :], x_in[:, i, :],
                                                       mean_var[:, i, 0:1], ln[:, 1, i:i + 1],
                                                       ALU.subtract, ALU.mult)
                    last.then_inc(xn_ready, 1)
                elif kind in ("TL", "KL", "KN", "QL"):
                    n = count.p0(kind if kind == "KN" else kind[0], key)
                    dve.wait_ge(p0_hi, 2 * n + 2)
                    p0_bank = p0_banks[n % len(p0_banks)]
                    if kind == "TL":
                        b, c, half = key
                        tok = slice(half * HALF, (half + 1) * HALF)
                        nc.vector.tensor_tensor(xT_lo[:, c, tok], p0_bank,
                                                xT_hi[:, c, tok].bitcast(F32),
                                                ALU.subtract).then_inc(p0_free, 1)
                    elif kind == "KL":
                        par, tok = key[0] % 2, slice(key[1] * HALF, (key[1] + 1) * HALF)
                        nc.vector.tensor_tensor(k_hilo[par][LATENT:P, tok], p0_bank[LATENT:P, :],
                                                k_hilo[par][LATENT:P, tok].bitcast(F32),
                                                ALU.subtract).then_inc(p0_free, 1)
                    elif kind == "KN":
                        dve.sem_inc(p0_free, 1)
                    elif kind == "QL":
                        seg, j = key
                        for g in range(2):
                            rows = slice(g * LATENT, (g + 1) * LATENT)
                            last = nc.vector.tensor_tensor(
                                q_lo[seg % 2][0:LATENT, 2 * j + g, :], p0_bank[rows, :],
                                q_hi[seg % 2][rows, 2 * j + g, :].bitcast(F32), ALU.subtract)
                        last.then_inc(p0_free, 1)

        def gpsimd_program(pool, plan):
            count = Count(plan)
            for kind, key in plan:
                if kind != "ST":
                    continue
                t, unit, s, g = key
                slot = t % PT_SLOTS
                part = slice(g * BANK, (g + 1) * BANK)
                pool.wait_ge(exp_done, 2 * t + g + 1)
                if s == 0:
                    v = probs[:, slot, part].rearrange("p (h q) -> p h q", q=P)
                    nc.gpsimd.affine_select(
                        out=v, in_=v, pattern=[[0, 4], [1, P]], compare_op=ALU.is_ge, fill=0.0,
                        base=0, channel_multiplier=-1).then_inc(pool_done, 1)
                    continue
                sums = p_sum[:, unit % SUM_SLOTS, part]
                if s == 1:
                    if g == 0 and unit >= SUM_SLOTS:
                        pool.wait_ge(p1_full, count.p1("R", unit - SUM_SLOTS) + 1)
                    other = probs[:, (t - 1) % PT_SLOTS, part]
                else:
                    other = sums
                pool.wait_ge(pool_done, 2 * t + g - 1)
                nc.gpsimd.tensor_tensor(sums, other, probs[:, slot, part],
                                        ALU.add).then_inc(pool_done, 1)

        x_by_turn = x.rearrange("(t n) l d -> t n l d", n=IN_BODY)
        out_by_turn = out.rearrange("(t n) l d -> t n l d", n=IN_BODY)

        def sync_program(sp, plan, turn):
            count = Count(plan)
            for kind, key in plan:
                if kind == "Q":
                    seg, j = key
                    sp.wait_ge(p0_hi, 2 * count.p0(kind, key) + 2)
                    top, low = slice(0, LATENT), slice(LATENT, P)
                    buf = q_hi[seg % 2]
                    sp.dma_start(buf[low, 2 * j, :].bitcast(F32),
                                 buf[top, 2 * j, :].bitcast(F32)).then_inc(q_twice[j], 16)
                    sp.dma_start(buf[top, 2 * j + 1, :].bitcast(F32),
                                 buf[low, 2 * j + 1, :].bitcast(F32)).then_inc(q_twice[j], 16)
                elif kind == "MT":
                    n = count.of(kind, key)
                    sp.wait_ge(p1_free, count.p1(kind, key) + 1)
                    row = q_lo[key // 4 % 2][LATENT:LATENT + 1, :, columns(key)]
                    sp.dma_start(row.bitcast(F32),
                                 neg_rows[:, n % 4, :].bitcast(F32)).then_inc(row_placed[n % 4], 16)
                elif kind == "O" and octet_of(key) == 1:
                    i = block_of(key)
                    sp.wait_ge(p1_free, count.p1(kind, key) + 1)
                    sp.dma_start(out_by_turn[turn, key // UNITS, i * P:(i + 1) * P, :],
                                 acc[:, i, :]).then_inc(stored[segment_kind(i)], 16)
                elif kind == "X":
                    sp.wait_ge(ff_added, BLOCKS * key)
                    at = (turn + key // IN_BODY) % (B // IN_BODY) if key >= IN_BODY else turn
                    nxt = x_by_turn[at, key % IN_BODY]
                    sp.dma_start(x_in[:, :, :], nxt.rearrange("(i p) d -> p i d", p=P)
                                 ).then_inc(x_loaded, 16)
            for j in range(PAIRS):
                sp.wait_ge(q_twice[j], 32 * sum(k == "Q" and key[1] == j for k, key in plan))
            turned = sum(k == "MT" for k, _ in plan)
            for i in range(min(4, turned)):
                sp.wait_ge(row_placed[i], 16 * ((turned - i + 3) // 4))
            outputs = sum(k == "O" and octet_of(u) == 1 for k, u in plan)
            if outputs:
                for s in range(2):
                    sp.wait_ge(stored[s], 16 * outputs // 2)

        def run(plan, turn, p0_banks, load=None, make_constants=None):
            with nc.Block() as block:
                @block.tensor
                def _(pe):
                    tensor_program(pe, plan, p0_banks)

                @block.scalar
                def _(act):
                    scalar_program(act, plan, p0_banks)

                @block.vector
                def _(dve):
                    vector_program(dve, plan, p0_banks)

                @block.gpsimd
                def _(pool):
                    if make_constants:
                        make_constants(pool)
                    gpsimd_program(pool, plan)

                @block.sync
                def _(sp):
                    if load:
                        load(sp)
                    sync_program(sp, plan, turn)

            nc.all_engine_barrier(sems_to_clear=range(names[0].num, names[-1].num + 1))

        run(first_plan(), 0, [ps[:, 6, :], ps[:, 0, :], ps[:, 1, :]], load_all, make_constants)
        plan = body_plan(IN_BODY)
        with nc.Fori(0, B // IN_BODY) as turn:
            run(plan, turn, [ps[:, 6, :]])


_INS = ["L0_attn_x_bld", "L0_attn_Wq", "L0_attn_Wkv_down", "L0_attn_Wk_up", "L0_attn_Wv_up",
        "L0_attn_Wout", "L0_ffn_weight", "L0_ffn_aux_weight1", "L0_ffn_aux_weight2", "L0_ffn_bias"]


def kernel(**inputs):
    import numpy as np
    import concourse.bacc as bacc
    from concourse.bass_utils import run_bass_kernel_spmd

    nc = bacc.Bacc("TRN2", target_bir_lowering=False, num_devices=1)
    arrays, args = {}, []
    for name in _INS:
        a = np.ascontiguousarray(inputs[name])
        arrays[f"in_{name}"] = a
        args.append(nc.dram_tensor(f"in_{name}", a.shape, F32, kind="ExternalInput").ap())
    shape = arrays["in_L0_attn_x_bld"].shape
    args.append(nc.dram_tensor("out_x", shape, F32, kind="ExternalOutput").ap())
    build(nc, *args)
    result = run_bass_kernel_spmd(nc, [arrays], core_ids=[0])
    return result.results[0]["out_x"]
```
